# Optimizing a Trainium2 kernel written in Bass

```python
import numpy as np
import jax
import jax.numpy as jnp

def _softmax(x, axis=-1):
    return jax.nn.softmax(x, axis=axis)

def _gelu(x):
    return jax.nn.gelu(x, approximate=True)

def _silu(x):
    return jax.nn.silu(x)

def _sigmoid(x):
    return jax.nn.sigmoid(x)

def _layernorm(x, axis=-1, eps=1e-05):
    m = jnp.mean(x, axis=axis, keepdims=True)
    v = jnp.var(x, axis=axis, keepdims=True)
    return (x - m) / jnp.sqrt(v + eps)

def _scatter_add(tgt, idx, src, axis=0):
    return tgt.at[idx].add(src)

def _segment_sum(src, seg, n):
    return jax.ops.segment_sum(src, seg, n)
kernel_name = 'mk_gnn_resnorm_d1_gnn_r8_349c8b'

def setup_inputs(seed: int=0):
    np.random.seed(seed)
    _w = jnp.asarray

    def _rec_inputs():
        import jax
        import jax.numpy as jnp
        _gk = jax.random.key(seed)
        x = -0.0005121 + 1.001 * jax.random.normal(jax.random.fold_in(_gk, 1), (12500, 32), jnp.float32)
        src = jax.random.randint(jax.random.fold_in(_gk, 2), (200000,), 0, 12500, jnp.int32)
        dst = jax.random.randint(jax.random.fold_in(_gk, 3), (200000,), 0, 12500, jnp.int32)
        _o = jnp.argsort(dst, stable=True)
        src = src[_o]
        dst = dst[_o]
        edge_attr_4 = 0.000398945 + 1.00003 * jax.random.normal(jax.random.fold_in(_gk, 11), (200000, 4), jnp.float32)
        return (x, src, dst, edge_attr_4)
    x, src, dst, edge_attr_4 = _rec_inputs()

    def _L0_gnn_setup():
        import jax, jax.numpy as jnp
        import numpy as np
        N_NODES = 12500
        N_EDGES = 200000
        IN_DIM = 32
        HID = 64
        OUT_DIM = 32
        EDGE_DIM = 4
        key = jax.random.key(seed)
        ks = jax.random.split(key, 12)
        x = jax.random.normal(ks[0], (N_NODES, IN_DIM), dtype=jnp.float32)
        edge_index = jax.random.randint(ks[1], (2, N_EDGES), 0, N_NODES, dtype=jnp.int32)
        edge_attr = jax.random.normal(ks[2], (N_EDGES, EDGE_DIM), dtype=jnp.float32)

        def lin(k, fan_in, fan_out):
            kw, kb = jax.random.split(k)
            bound = 1.0 / np.sqrt(fan_in)
            W = jax.random.uniform(kw, (fan_in, fan_out), minval=-bound, maxval=bound, dtype=jnp.float32)
            b = jax.random.uniform(kb, (fan_out,), minval=-bound, maxval=bound, dtype=jnp.float32)
            return (W, b)
        W1, b1 = lin(ks[3], 2 * IN_DIM, HID)
        W2, b2 = lin(ks[4], HID, 2 * HID)
        W3, b3 = lin(ks[5], 2 * HID, HID)
        W4, b4 = lin(ks[6], HID, OUT_DIM)
        return {'x': x, 'edge_index': edge_index, 'edge_attr': edge_attr, 'W1': W1, 'b1': b1, 'W2': W2, 'b2': b2, 'W3': W3, 'b3': b3, 'W4': W4, 'b4': b4}
    _L0_gnn_all = _L0_gnn_setup()
    _L0_gnn_in = {k: v for k, v in _L0_gnn_all.items() if k in ('W1', 'b1', 'W2', 'b2', 'W3', 'b3', 'W4', 'b4')}
    del _L0_gnn_all
    return {'x': x, 'src': src, 'dst': dst, 'edge_attr_4': edge_attr_4, 'L0_gnn_W1': _L0_gnn_in['W1'], 'L0_gnn_b1': _L0_gnn_in['b1'], 'L0_gnn_W2': _L0_gnn_in['W2'], 'L0_gnn_b2': _L0_gnn_in['b2'], 'L0_gnn_W3': _L0_gnn_in['W3'], 'L0_gnn_b3': _L0_gnn_in['b3'], 'L0_gnn_W4': _L0_gnn_in['W4'], 'L0_gnn_b4': _L0_gnn_in['b4']}

def reference(x, src, dst, edge_attr_4, L0_gnn_W1, L0_gnn_b1, L0_gnn_W2, L0_gnn_b2, L0_gnn_W3, L0_gnn_b3, L0_gnn_W4, L0_gnn_b4):
    import jax
    import jax.numpy as jnp

    def _L0_gnn_ref(x, edge_index, edge_attr, W1, b1, W2, b2, W3, b3, W4, b4):
        import jax, jax.numpy as jnp
        import numpy as np
        N_NODES = 12500
        N_EDGES = 200000
        IN_DIM = 32
        HID = 64
        OUT_DIM = 32
        EDGE_DIM = 4
        j_idx = edge_index[0]
        i_idx = edge_index[1]
        x_j = x[j_idx]
        x_i = x[i_idx]
        msg = jnp.concatenate([x_i, x_j - x_i], axis=-1)
        h = jax.nn.relu(msg @ W1 + b1)
        h = jax.nn.relu(h @ W2 + b2)
        h = jax.nn.relu(h @ W3 + b3)
        m = h @ W4 + b4
        s = jax.ops.segment_sum(m, i_idx, num_segments=N_NODES)
        cnt = jax.ops.segment_sum(jnp.ones((m.shape[0],), m.dtype), i_idx, num_segments=N_NODES)
        return s / jnp.maximum(cnt, 1.0)[:, None]
    edge_index = jnp.stack([src, dst])
    x = _layernorm(x + _L0_gnn_ref(x, edge_index, edge_attr_4, L0_gnn_W1, L0_gnn_b1, L0_gnn_W2, L0_gnn_b2, L0_gnn_W3, L0_gnn_b3, L0_gnn_W4, L0_gnn_b4), axis=-1)
    return x

_drawn_inputs = setup_inputs


def setup_inputs(seed=0):
    import zlib

    import numpy as np

    out = dict(_drawn_inputs(seed))
    spreads = {}
    factors = {'L0_gnn_W1': 2.815, 'L0_gnn_b1': 8.0, 'L0_gnn_b2': 5.433, 'L0_gnn_b3': 2.688}
    for name, (base, spread) in spreads.items():
        noise = np.random.default_rng([zlib.crc32(name.encode()), seed]).standard_normal(out[name].shape)
        drawn = base * np.exp(spread * noise) if base else spread * noise
        out[name] = jnp.asarray(drawn.astype(out[name].dtype))
    for name, factor in factors.items():
        out[name] = (out[name] * factor).astype(out[name].dtype)
    return out
```

```python
import concourse.bass as bass
from concourse import mybir
from contextlib import ExitStack

F32 = mybir.dt.float32
BF16 = mybir.dt.bfloat16
I32 = mybir.dt.int32
ALU = mybir.AluOpType
ACT = mybir.ActivationFunctionType
AX = mybir.AxisListType

N, E = 12500, 200000
D, H1, H2, H3 = 32, 64, 128, 64
O = 32
P = 128
EPS = 1e-5

T = P
J = 4
GE = J * T
G = -(-E // GE)
TILES = G * J
FULL = E // T
HALF = E - FULL * T
BLK = TILES // P
REST = TILES - BLK * P
WIN = P // 3
K3 = 3 * WIN
NPAD = N + WIN
R = 4
LOOPS = (G - R) // R
NP = 125
NC = N // NP
CH = 15
CHUNKS = [(c, min(CH, NC - c)) for c in range(0, NC, CH)]

C_ID, C_IOTA, C_PMOD, C_MASK, C_DIG, C_END = 0, P, P + J * WIN, P + J * WIN + 1, P + J * WIN + 4, P + J * WIN + 4 + K3


def build(nc, x, src, dst, W1, b1, W2, b2, W3, b3, W4, b4, consts, out):
    assert HALF * 2 == T and FULL == TILES - 2 and NP * NC == N
    ctx = ExitStack()
    with ctx:
        def sb(name, shape, dt):
            return ctx.enter_context(nc.sbuf_tensor(name, shape, dt))

        def sem(name):
            return ctx.enter_context(nc.semaphore(name))

        x_parts = nc.dram_tensor("x_parts", (3, NPAD, D), BF16, kind="Internal").ap()
        dst_digits = nc.dram_tensor("dst_digits", (2, TILES * T), BF16, kind="Internal").ap()

        cst = sb("cst", [P, C_END], F32)
        ident = cst[:, C_ID:C_ID + P]
        digit_w = sb("digit_w", [2, K3], BF16)
        ones3 = sb("ones3", [3, P], BF16)
        node_off = sb("node_off", [P, 1], F32)
        w1cat = sb("w1cat", [P, P], F32)
        w1sub = sb("w1sub", [2 * D, H1], F32)
        w2s = sb("w2s", [P, H2], F32)
        w3s = sb("w3s", [H2, H3], F32)
        w4s = sb("w4s", [H3 + 1, O + 1], F32)
        b1s = sb("b1s", [H1, 1], F32)
        b2s = sb("b2s", [H2, 1], F32)
        b3s = sb("b3s", [3, H3], F32)
        b3r = sb("b3r", [3, 2, H3], F32)
        b3p = sb("b3p", [3, 3, H3], BF16)
        b3m = sb("b3m", [3, H3], BF16)

        src_i = sb("src_i", [P, BLK + 1, T], I32)
        dst_i = sb("dst_i", [P, BLK + 1, T], I32)
        edge_f = sb("edge_f", [P, 2, BLK + 1, T], F32)
        src_f, dst_f = edge_f[:, 0, :, :], edge_f[:, 1, :, :]
        dig_i = sb("dig_i", [P, 2, BLK + 1, T], I32)
        dig_b = sb("dig_b", [P, 2, BLK + 1, T], BF16)
        tile_min = sb("tile_min", [P, BLK + 1], F32)
        tile_max = sb("tile_max", [P, BLK + 1], F32)
        diag = sb("diag", [P, 2, BLK + 1, T], F32)
        diag_min, diag_max = diag[:, 0, :, :], diag[:, 1, :, :]
        ones = sb("ones", [P, P], F32)
        src_t = sb("src_t", [P, TILES], I32)
        dst_t = sb("dst_t", [P, TILES], F32)
        dst_rel = dst_t[:, :].rearrange("p (g j) -> p g j", j=J)
        neg_base = sb("neg_base", [P, G], F32)
        span = sb("span", [P, G], F32)
        widest = sb("widest", [P, 1], F32)
        passes_end = sb("passes_end", [1, 1], I32)
        base_f = sb("base_f", [1, G], F32)
        base_i = sb("base_i", [1, G], I32)

        x_nat = sb("x_nat", [NP, NC * D], F32)
        x_res = sb("x_res", [NP, NC * D], F32)
        x_p = sb("x_p", [NP, 3, NC * D], BF16)
        zpad = sb("zpad", [WIN, 3, D], BF16)
        sums = sb("sums", [H3 + 1, NPAD], F32)

        idx = sb("idx", [P, R, J], I32)
        xj = sb("xj", [P, R, J, D], F32)
        xwin = sb("xwin", [K3, R, D], BF16)
        dig = sb("dig", [2, R, GE], BF16)
        pick = sb("pick", [K3, 2, GE], BF16)
        onehot = sb("onehot", [P, 2, J, WIN], F32)
        xcat = sb("xcat", [P, 2, GE], F32)
        h1 = sb("h1", [P, 2, GE], F32)
        h2 = sb("h2", [H2, 2, GE], F32)
        h3 = sb("h3", [P, 2, J, H3 + 1], F32)

        def last(v):
            return v[:, 0:NC * O].rearrange("p (c f) -> p c f", f=O)

        cnt = sb("cnt", [NP, NC], F32)
        rcnt = sb("rcnt", [NP, NC], F32)
        z = last(x_res[:, :])
        zc = last(edge_f[0:NP, :, :, :].rearrange("p a b e -> p (a b e)"))
        zq = last(dig_i[0:NP, :, :, :].rearrange("p a b e -> p (a b e)").bitcast(F32))
        mean = sb("mean", [NP, NC], F32)
        var = sb("var", [NP, NC], F32)
        std = sb("std", [NP, NC], F32)
        rstd = sb("rstd", [NP, NC], F32)
        eps = sb("eps", [NP, 1], F32)
        y = last(diag[0:NP, :, :, :].rearrange("p a b e -> p (a b e)"))

        ps = ctx.enter_context(nc.psum_tensor("ps", [P, 8, 512], F32))
        psf = ps[:, :, :].rearrange("p b n -> p (b n)")
        p_dst = ps[0:K3, 0, :]
        p_xc = ps[0:2 * D, 1, :]
        p_h1 = ps[:, 2, :]
        p_h2 = ps[:, 3, :]
        p_h3 = ps[:, 4, 0:J * H3]
        p_agg = ps[0:H3 + 1, 5, 0:WIN]
        p_iota = ps[:, 6, 0:J * WIN]

        s_src, s_dst, s_cst = sem("src_in"), sem("dst_in"), sem("cst_in")
        s_x, s_w = sem("x_in"), sem("weights_in")
        s_srcf, s_dstf = sem("src_as_float"), sem("dst_as_float")
        s_srcT, s_dstT, s_dstTc, s_idx = sem("src_transposed"), sem("dst_transposed"), sem("dst_columns"), sem("indices")
        s_diag, s_minb, s_maxb, s_base = sem("diagonals"), sem("tile_min_spread"), sem("tile_max_spread"), sem("bases")
        s_digi, s_digb, s_digst = sem("digits_int"), sem("digits_bf16"), sem("digits_stored")
        s_hi, s_mid, s_parts, s_xpst = sem("x_hi"), sem("x_mid"), sem("x_parts_ready"), sem("x_parts_stored")
        s_res1, s_res2 = sem("x_minus_hi"), sem("x_minus_hi_mid")
        s_wz = sem("zero_rows_set")
        s_set, s_w4z = sem("constants_set"), sem("w4_zeroed")
        s_vc = sem("vector_chain")
        s_fin, s_rc, s_z, s_zc, s_sq, s_var, s_std, s_rstd, s_y, s_out = (
            sem("final_product"), sem("z_free"), sem("z_ready"), sem("z_centred"), sem("z_squared"), sem("var_ready"),
            sem("std_ready"), sem("rstd_ready"), sem("y_ready"), sem("out_stored"))

        s_gath = [sem(f"gathered{u}") for u in range(R)]
        s_xwin = [sem(f"window_in{u}") for u in range(R)]
        s_dig = [sem(f"digits_in{u}") for u in range(R)]
        s_pd, s_px, s_l1, s_l2, s_l3, s_agg = (sem("dst_spread"), sem("x_in_psum"), sem("layer1"), sem("layer2"),
                                               sem("layer3"), sem("window_summed"))
        s_stage = sem("indices_staged")
        s_begun = sem("gathers_begun")
        s_pick, s_oh, s_xc, s_acc = sem("pick_built"), sem("onehot_built"), sem("x_copied"), sem("sums_added")
        s_r1, s_r2, s_r3 = sem("relu1"), sem("relu2"), sem("relu3")
        s_arrive = sem("pass_arrived")
        per_pass = [*s_gath, *s_xwin, *s_dig, s_pd, s_px, s_l1, s_l2, s_l3, s_agg, s_stage, s_begun, s_pick, s_oh, s_xc, s_acc,
                    s_r1, s_r2, s_r3, s_arrive]
        s_open = sem("pass_open")

        block = ctx.enter_context(nc.Block())

        def rows_of(v):
            return (v[0:BLK * P * T].rearrange("(b p e) -> p b e", p=P, e=T),
                    v[BLK * P * T:FULL * T].rearrange("(p e) -> p e", e=T))

        def end_of_pass(eng, off):
            eng.sem_inc(s_arrive, 1)
            eng.wait_ge(s_open, off + WIN)

        def normalise(pool, n):
            c0, w = CHUNKS[n]
            at = slice(c0, c0 + w)
            pool.wait_ge(s_rstd, n + 1)
            pool.wait_ge(s_zc, n + 1)
            nc.gpsimd.tensor_tensor(y[:, at, :], zc[:, at, :], rstd[:, at].unsqueeze(2).to_broadcast([NP, w, O]),
                                    ALU.mult).then_inc(s_y, 1)

        def root(act, n):
            c0, w = CHUNKS[n]
            act.wait_ge(s_var, n + 1)
            nc.scalar.activation(std[:, c0:c0 + w], var[:, c0:c0 + w], ACT.Sqrt, bias=eps[:, 0:1],
                                 scale=1.0 / O).then_inc(s_std, 1)

        def variance(dve, n):
            c0, w = CHUNKS[n]
            dve.wait_ge(s_sq, n + 1)
            nc.vector.tensor_reduce(var[:, c0:c0 + w], zq[:, c0:c0 + w, :], AX.X, ALU.add).then_inc(s_var, 1)

        def inverse(dve, n):
            c0, w = CHUNKS[n]
            dve.wait_ge(s_std, n + 1)
            nc.vector.reciprocal(rstd[:, c0:c0 + w], std[:, c0:c0 + w]).then_inc(s_rstd, 1)

        @block.sync
        def _(sp):
            for v, t, s in ((src, src_i, s_src), (dst, dst_i, s_dst)):
                full, rest = rows_of(v)
                half = v[FULL * T:E].rearrange("(a e) -> a e", a=1)
                sp.dma_start(t[:, 0:BLK, :], full).then_inc(s, 16)
                sp.dma_start(t[0:REST - 2, BLK, :], rest).then_inc(s, 16)
                for k in (REST - 2, REST - 1):
                    for h in (0, HALF):
                        sp.dma_start(t[k:k + 1, BLK, h:h + HALF], half).then_inc(s, 16)
                if v is src:
                    sp.dma_start(cst[:, :], consts).then_inc(s_cst, 16)
            sp.wait_ge(s_wz, 1)
            sp.dma_start(w1cat[0:D, 0:H1], W1[D:2 * D, :]).then_inc(s_w, 16)
            sp.dma_start(w1cat[D:2 * D, 0:H1], W1[0:D, :]).then_inc(s_w, 16)
            sp.dma_start(w1sub[D:2 * D, :], W1[D:2 * D, :]).then_inc(s_w, 16)
            sp.dma_start(w2s[0:H1, :], W2).then_inc(s_w, 16)
            sp.dma_start(w3s[:, :], W3).then_inc(s_w, 16)
            sp.dma_start(b1s[:, :], b1.rearrange("(n a) -> n a", a=1)).then_inc(s_w, 16)
            sp.dma_start(b2s[:, :], b2.rearrange("(n a) -> n a", a=1)).then_inc(s_w, 16)
            for k in range(3):
                sp.dma_start(b3s[k:k + 1, :], b3.rearrange("(a n) -> a n", a=1)).then_inc(s_w, 16)
            sp.wait_ge(s_w4z, 2)
            sp.dma_start(w4s[0:H3, 0:O], W4).then_inc(s_w, 16)
            sp.dma_start(w4s[H3:H3 + 1, 0:O], b4.rearrange("(a n) -> a n", a=1)).then_inc(s_w, 16)
            sp.wait_ge(s_digb, 4)
            for d in range(2):
                row = dst_digits[d, :]
                sp.dma_start(row[0:BLK * P * T].rearrange("(b p e) -> p b e", p=P, e=T),
                             dig_b[:, d, 0:BLK, :]).then_inc(s_digst, 16)
                sp.dma_start(row[BLK * P * T:TILES * T].rearrange("(p e) -> p e", e=T),
                             dig_b[0:REST, d, BLK, :]).then_inc(s_digst, 16)
            sp.wait_ge(s_parts, 1)
            sp.wait_ge(s_mid, 1)
            sp.wait_ge(s_hi, 1)
            sp.wait_ge(s_set, 1)
            for k in range(3):
                sp.dma_start(x_parts[k, 0:N, :].rearrange("(p c) f -> p (c f)", p=NP), x_p[:, k, :]).then_inc(s_xpst, 16)
                sp.dma_start(x_parts[k, N:NPAD, :], zpad[:, k, :]).then_inc(s_xpst, 16)
            sp.wait_ge(s_digst, 4 * 16)
            sp.wait_ge(s_xpst, 6 * 16)
            sp.wait_ge(s_base, 1)
            end = sp.value_load(passes_end[0:1, 0:1], min_val=1, max_val=N)

            def load(g, u):
                if not (isinstance(g, int) and g < R):
                    sp.wait_ge(s_px, g - R + 1)
                col = g if isinstance(g, int) else bass.ds(g, 1)
                col = base_i[0:1, g:g + 1] if isinstance(g, int) else base_i[0:1, col]
                first = sp.value_load(col, min_val=0, max_val=N)
                sp.dma_start(xwin[:, u, :], x_parts[:, bass.ds(first, WIN), :]).then_inc(s_xwin[u], 16)
                at = slice(g * GE, (g + 1) * GE) if isinstance(g, int) else bass.ds(g * GE, GE)
                sp.dma_start(dig[:, u, :], dst_digits[:, at]).then_inc(s_dig[u], 16)

            with sp.Fori(0, end, WIN) as off:
                for g in range(R):
                    load(g, g)
                with sp.Fori(1, LOOPS) as i:
                    for u in range(R):
                        load(i * R + u, u)
                for g in range(LOOPS * R, G):
                    load(g, g % R)
                sp.wait_ge(s_acc, G)
                sp.wait_ge(s_arrive, 4)
                for s in per_pass:
                    sp.sem_clear(s)
                sp.sem_inc(s_open, WIN)

            for n, (c0, w) in enumerate(CHUNKS):
                sp.wait_ge(s_y, n + 1)
                sp.dma_start(out.rearrange("(p c) f -> p c f", p=NP)[:, c0:c0 + w, :], y[:, c0:c0 + w, :]).then_inc(s_out, 16)
            sp.wait_ge(s_out, 16 * len(CHUNKS))

        @block.gpsimd
        def _(pool):
            nc.gpsimd.memset(zpad[:, :, :], 0.0).then_inc(s_set, 1)
            nc.gpsimd.memset(sums[:, :], 0.0).then_inc(s_set, 1)
            nc.gpsimd.memset(h3[:, :, :, :], 1.0).then_inc(s_set, 1)
            nc.gpsimd.memset(w4s[:, :], 0.0).then_inc(s_w4z, 1)
            pool.wait_ge(s_w4z, 1)
            nc.gpsimd.memset(w4s[H3:H3 + 1, O:O + 1], 1.0).then_inc(s_w4z, 1)

            def gather(g, u):
                pool.wait_ge(s_stage, g + 1)
                pool.sem_inc(s_begun, 1)
                for j in range(J):
                    if isinstance(g, int) and g * J + j == TILES - 1:
                        break
                    pool.indirect_dma_start(out=xj[:, u, j, :], out_offset=None, in_=x,
                                            in_offset=bass.IndirectOffsetOnAxis(ap=idx[:, u, j:j + 1], axis=0))\
                        .then_inc(s_gath[u], 16)

            for g in range(R):
                gather(g, g)
            pool.wait_ge(s_base, 1)
            end = pool.value_load(passes_end[0:1, 0:1], min_val=1, max_val=N)
            with pool.Fori(0, end, WIN) as off:
                with pool.Fori(1, LOOPS) as i:
                    for u in range(R):
                        gather(i * R + u, u)
                for g in range(LOOPS * R, G):
                    gather(g, g % R)
                for u in range(R):
                    pool.wait_ge(s_gath[u], 16 * sum(1 for t in range(TILES - 1) if t // J % R == u))
                pool.dma_reset(range(s_gath[0].num, s_gath[-1].num + 1))
                end_of_pass(pool, off)
                pool.sem_inc(s_begun, 1)
                with pool.If(off + WIN < end):
                    for g in range(R):
                        gather(g, g)

            for n, (c0, w) in enumerate(CHUNKS):
                at = slice(c0, c0 + w)
                pool.wait_ge(s_z, n + 1)
                nc.gpsimd.tensor_tensor(zc[:, at, :], z[:, at, :],
                                        mean[:, at].unsqueeze(2).to_broadcast([NP, w, O]),
                                        ALU.subtract).then_inc(s_zc, 1)
                if n >= 1:
                    normalise(pool, n - 1)
            normalise(pool, len(CHUNKS) - 1)


        @block.scalar
        def _(act):
            act.dma_start(x_nat[:, :], x.rearrange("(p c) f -> p (c f)", p=NP)).then_inc(s_x, 16)
            act.wait_ge(s_srcT, BLK + 1)
            for b in range(4):
                n = min(512, TILES - 512 * b)
                nc.scalar.activation(src_t[:, 512 * b:512 * b + n], ps[:, b, 0:n], ACT.Copy).then_inc(s_idx, 1)
            act.wait_ge(s_dstT, BLK + 1)
            for b in range(4):
                n = min(512, TILES - 512 * b)
                nc.scalar.activation(dst_t[:, 512 * b:512 * b + n], ps[:, 4 + b, 0:n], ACT.Copy).then_inc(s_dstTc, 1)
            act.wait_ge(s_digi, 4)
            for d in range(2):
                nc.scalar.activation(dig_b[:, d, 0:BLK, :], dig_i[:, d, 0:BLK, :], ACT.Copy).then_inc(s_digb, 1)
                nc.scalar.activation(dig_b[0:REST, d, BLK, :], dig_i[0:REST, d, BLK, :], ACT.Copy).then_inc(s_digb, 1)
            act.wait_ge(s_x, 16)
            nc.scalar.activation(x_p[:, 0, :], x_nat[:, :], ACT.Copy).then_inc(s_hi, 1)
            act.wait_ge(s_res1, 1)
            nc.scalar.activation(x_p[:, 1, :], x_res[:, :], ACT.Copy).then_inc(s_mid, 1)
            act.wait_ge(s_w, 12 * 16)
            act.wait_ge(s_set, 3)
            act.wait_ge(s_base, 1)
            end = act.value_load(passes_end[0:1, 0:1], min_val=1, max_val=N)

            def static_below(g, n):
                return isinstance(g, int) and g < n

            def relu1(g, v):
                act.wait_ge(s_l1, g + 1)
                if not static_below(g, 2):
                    act.wait_ge(s_l2, g - 1)
                nc.scalar.activation(h1[0:H1, v, :], p_h1[0:H1, :], ACT.Relu, bias=b1s[:, 0:1]).then_inc(s_r1, 1)

            def relu2(g, v):
                act.wait_ge(s_l2, g + 1)
                if not static_below(g, 2):
                    act.wait_ge(s_l3, g - 1)
                nc.scalar.activation(h2[:, v, :], p_h2, ACT.Relu, bias=b2s[:, 0:1]).then_inc(s_r2, 1)

            def relu3(g, v):
                act.wait_ge(s_l3, g + 1)
                if not static_below(g, 2):
                    act.wait_ge(s_agg, g - 1)
                nc.scalar.activation(h3[:, v, :, 0:H3], p_h3.rearrange("p (j f) -> p j f", j=J),
                                     ACT.Relu).then_inc(s_r3, 1)

            def step(s, u, last=False):
                first = isinstance(s, int) and s == 0
                if not first:
                    relu2(s - 1, (u - 1) % 2)
                if not last:
                    relu1(s, u % 2)
                if not first:
                    relu3(s - 1, (u - 1) % 2)

            with act.Fori(0, end, WIN) as off:
                for s in range(R):
                    step(s, s)
                with act.Fori(1, LOOPS) as i:
                    for u in range(R):
                        step(i * R + u, u)
                for s in range(LOOPS * R, G + 1):
                    step(s, s % R, last=s == G)
                end_of_pass(act, off)

            for n, (c0, w) in enumerate(CHUNKS):
                at = slice(c0, c0 + w)
                act.wait_ge(s_zc, n + 1)
                nc.scalar.activation(zq[:, at, :], zc[:, at, :], ACT.Square).then_inc(s_sq, 1)
                if n >= 1:
                    root(act, n - 1)
            root(act, len(CHUNKS) - 1)


        @block.tensor
        def _(pe):
            pe.wait_ge(s_cst, 16)
            pe.wait_ge(s_srcf, 2)
            for b in range(BLK + 1):
                k = P if b < BLK else REST
                nc.tensor.transpose(ps[:, b // 4, b % 4 * P:b % 4 * P + k], src_f[0:k, b, :], ident[0:k, 0:k]).then_inc(s_srcT, 1)
            pe.wait_ge(s_dstf, 2)
            for b in range(BLK + 1):
                k = P if b < BLK else REST
                nc.tensor.transpose(ps[:, 4 + b // 4, b % 4 * P:b % 4 * P + k], dst_f[0:k, b, :], ident[0:k, 0:k]).then_inc(s_dstT, 1)
            for n, (diag, bank, free, s) in enumerate(((diag_min, 0, s_idx, s_minb), (diag_max, 4, s_dstTc, s_maxb))):
                pe.wait_ge(s_diag, 5 if n == 0 else 6)
                pe.wait_ge(free, 4)
                for b in range(BLK + 1):
                    k = P if b < BLK else REST
                    nc.tensor.matmul(ps[:, bank + b // 4, b % 4 * P:b % 4 * P + k], ones[0:k, :], diag[0:k, b, 0:k],
                                     start=True, stop=True).then_inc(s, 1)
            pe.wait_ge(s_base, 1)
            end = pe.value_load(passes_end[0:1, 0:1], min_val=1, max_val=N)
            pe.wait_ge(s_w, 12 * 16)
            pe.wait_ge(s_wz, 4)

            def static_below(g, n):
                return isinstance(g, int) and g < n

            def spread_dst(g, u):
                pe.wait_ge(s_dig[u], turn(g, u, 16))
                if not static_below(g, 1):
                    pe.wait_ge(s_pick, g)
                nc.tensor.matmul(p_dst, digit_w[:, :], dig[:, u, :], start=True, stop=True).then_inc(s_pd, 1)

            def turn(g, u, n):
                return (g // R + 1) * n if isinstance(g, int) else (g - u + R) * (n // R)

            def collect_x(g, u, v):
                pe.wait_ge(s_gath[u], turn(g, u, 16 * J) - (16 if isinstance(g, int) and g == G - 1 else 0))
                pe.wait_ge(s_xwin[u], turn(g, u, 16))
                pe.wait_ge(s_pick, g + 1)
                if not static_below(g, 1):
                    pe.wait_ge(s_xc, g)
                for j in range(J):
                    nc.tensor.transpose(p_xc[0:D, j * T:(j + 1) * T], xj[:, u, j, :], ident)
                nc.tensor.matmul(p_xc[D:2 * D, :], xwin[:, u, :], pick[:, v, :], start=True, stop=True).then_inc(s_px, 1)

            def layer1(g, v):
                pe.wait_ge(s_xc, g + 1)
                if not static_below(g, 1):
                    pe.wait_ge(s_r1, g)
                nc.tensor.matmul(p_h1, w1cat[:, :], xcat[:, v, :], start=True, stop=True).then_inc(s_l1, 1)

            def layer2(g, v):
                pe.wait_ge(s_r1, g + 1)
                if not static_below(g, 1):
                    pe.wait_ge(s_r2, g)
                nc.tensor.matmul(p_h2, w2s[:, :], h1[:, v, :], start=True, stop=True).then_inc(s_l2, 1)

            def layer3(g, v):
                pe.wait_ge(s_r2, g + 1)
                if not static_below(g, 1):
                    pe.wait_ge(s_r3, g)
                for j in range(J):
                    part = p_h3[:, j * H3:(j + 1) * H3]
                    nc.tensor.matmul(part, ones3[:, :], b3m[:, :], start=True, stop=False)
                    last = nc.tensor.matmul(part, h2[:, v, j * T:(j + 1) * T], w3s[:, :], start=False, stop=True)
                last.then_inc(s_l3, 1)

            def sum_window(g, v):
                pe.wait_ge(s_r3, g + 1)
                pe.wait_ge(s_oh, g + 1)
                if not static_below(g, 1):
                    pe.wait_ge(s_acc, g)
                for j in range(J):
                    last = nc.tensor.matmul(p_agg, h3[:, v, j, :], onehot[:, v, j, :], start=j == 0, stop=j == J - 1)
                last.then_inc(s_agg, 1)

            def step(s, u):
                static = isinstance(s, int)
                if not static or s < G:
                    collect_x(s, u, u % 2)
                if not static or s >= 2:
                    sum_window(s - 2, u % 2)
                if not static or 1 <= s <= G:
                    layer2(s - 1, (u - 1) % 2)
                if not static or s < G:
                    layer1(s, u % 2)
                if not static or s + 1 < G:
                    spread_dst(s + 1, (u + 1) % R)
                if not static or 1 <= s <= G:
                    layer3(s - 1, (u - 1) % 2)

            with pe.Fori(0, end, WIN) as off:
                spread_dst(0, 0)
                for s in range(R):
                    step(s, s)
                with pe.Fori(1, LOOPS) as i:
                    for u in range(R):
                        step(i * R + u, u)
                for s in range(LOOPS * R, G + 2):
                    step(s, s % R)
                end_of_pass(pe, off)

            for n, (c0, w) in enumerate(CHUNKS):
                for c in range(w):
                    last = nc.tensor.matmul(ps[0:NP, n, c * (O + 1):(c + 1) * (O + 1)],
                                            sums[:, c0 + c:N:NC], w4s[:, :], start=True, stop=True)
                last.then_inc(s_fin, 1)

        @block.vector
        def _(dve):
            chain = [0]

            def at(g):
                return slice(g, g + 1) if isinstance(g, int) else bass.ds(g, 1)

            def stage_indices(g, u):
                nc.vector.tensor_copy(idx[:, u, :], src_t[:, :].rearrange("p (g j) -> p g j", j=J)[:, at(g), :]
                                      .rearrange("p a j -> p (a j)")).then_inc(s_stage, 1)

            def link(ins):
                chain[0] += 1
                ins.then_inc(s_vc, 1)
                dve.wait_ge(s_vc, chain[0])

            nc.vector.memset(w1cat[:, :], 0.0).then_inc(s_wz, 1)
            nc.vector.memset(w2s[H1:P, :], 0.0).then_inc(s_wz, 1)
            nc.vector.memset(xcat[2 * D:P, :, :], 0.0).then_inc(s_wz, 1)
            nc.vector.memset(h1[H1:P, :, :], 0.0).then_inc(s_wz, 1)
            dve.wait_ge(s_src, 6 * 16)
            nc.vector.tensor_copy(src_f[:, 0:BLK, :], src_i[:, 0:BLK, :]).then_inc(s_srcf, 1)
            nc.vector.tensor_copy(src_f[0:REST, BLK, :], src_i[0:REST, BLK, :]).then_inc(s_srcf, 1)
            dve.wait_ge(s_dst, 6 * 16)
            nc.vector.tensor_copy(dst_f[:, 0:BLK, :], dst_i[:, 0:BLK, :]).then_inc(s_dstf, 1)
            nc.vector.tensor_copy(dst_f[0:REST, BLK, :], dst_i[0:REST, BLK, :]).then_inc(s_dstf, 1)
            for d, (op, k) in enumerate(((ALU.arith_shift_right, 7), (ALU.bitwise_and, P - 1))):
                nc.vector.tensor_scalar(dig_i[:, d, 0:BLK, :], dst_i[:, 0:BLK, :], k, None, op).then_inc(s_digi, 1)
                nc.vector.tensor_scalar(dig_i[0:REST, d, BLK, :], dst_i[0:REST, BLK, :], k, None, op).then_inc(s_digi, 1)
            dve.wait_ge(s_dstf, 2)
            for t, op in ((tile_min, ALU.min), (tile_max, ALU.max)):
                nc.vector.tensor_reduce(t[:, 0:BLK], dst_f[:, 0:BLK, :], AX.X, op)
                link(nc.vector.tensor_reduce(t[0:REST, BLK:BLK + 1], dst_f[0:REST, BLK, :], AX.X, op))
            nc.vector.memset(ones[:, :], 1.0).then_inc(s_diag, 1)
            dve.wait_ge(s_cst, 16)
            for diag, t in ((diag_min, tile_min), (diag_max, tile_max)):
                nc.vector.tensor_tensor(diag[:, 0:BLK, :], ident.unsqueeze(1).to_broadcast([P, BLK, P]),
                                        t[:, 0:BLK].unsqueeze(2).to_broadcast([P, BLK, P]), ALU.mult).then_inc(s_diag, 1)
                nc.vector.tensor_scalar(diag[0:REST, BLK, :], ident[0:REST, :], t[0:REST, BLK:BLK + 1], None,
                                        ALU.mult).then_inc(s_diag, 1)
            nc.vector.memset(ones3[:, :], 1.0).then_inc(s_diag, 1)
            dve.wait_ge(s_hi, 1)
            nc.vector.tensor_tensor(x_res[:, :], x_nat[:, :], x_p[:, 0, :], ALU.subtract).then_inc(s_res1, 1)
            nc.vector.tensor_copy(digit_w[:, :], cst[0:2, C_DIG:C_DIG + K3])
            nc.vector.tensor_copy(node_off[:, :], cst[:, C_PMOD:C_PMOD + 1])
            nc.vector.memset(eps[:, :], EPS)
            dve.wait_ge(s_w, 12 * 16)
            nc.vector.tensor_tensor(w1cat[D:2 * D, 0:H1], w1cat[D:2 * D, 0:H1], w1sub[D:2 * D, :], ALU.subtract)
            link(nc.vector.tensor_copy(b3p[:, 0, :], b3s[:, :]))
            link(nc.vector.tensor_tensor(b3r[:, 0, :], b3s[:, :], b3p[:, 0, :], ALU.subtract))
            link(nc.vector.tensor_copy(b3p[:, 1, :], b3r[:, 0, :]))
            link(nc.vector.tensor_tensor(b3p[:, 2, :], b3r[:, 0, :], b3p[:, 1, :], ALU.subtract))
            link(nc.vector.tensor_scalar(b3r[:, 0, :], b3p[:, 0, :], cst[0:3, C_MASK:C_MASK + 1], None, ALU.mult))
            link(nc.vector.scalar_tensor_tensor(b3r[:, 1, :], b3p[:, 1, :], cst[0:3, C_MASK + 1:C_MASK + 2], b3r[:, 0, :],
                                                ALU.mult, ALU.add))
            link(nc.vector.scalar_tensor_tensor(b3r[:, 0, :], b3p[:, 2, :], cst[0:3, C_MASK + 2:C_MASK + 3], b3r[:, 1, :],
                                                ALU.mult, ALU.add))
            link(nc.vector.tensor_copy(b3m[:, :], b3r[:, 0, :]))
            dve.wait_ge(s_idx, 4)
            for g in range(R):
                stage_indices(g, g)
            dve.wait_ge(s_minb, BLK + 1)
            link(nc.vector.tensor_reduce(neg_base[:, :], psf[:, 0:TILES].rearrange("p (g j) -> p g j", j=J), AX.X,
                                         ALU.min, negate=True))
            link(nc.vector.tensor_scalar(base_f[:, :], neg_base[0:1, :], -1.0, None, ALU.mult))
            nc.vector.tensor_copy(base_i[:, :], base_f[:, :])
            dve.wait_ge(s_dstTc, 4)
            link(nc.vector.tensor_tensor(dst_rel[:, :, :], dst_t[:, :].rearrange("p (g j) -> p g j", j=J),
                                         neg_base[:, :].unsqueeze(2).to_broadcast([P, G, J]), ALU.add))
            nc.vector.memset(dst_rel[HALF:P, G - 1, J - 2:J - 1], -1.0)
            nc.vector.memset(dst_rel[:, G - 1, J - 1:J], -1.0)
            dve.wait_ge(s_maxb, BLK + 1)
            link(nc.vector.tensor_reduce(span[:, :], psf[:, 2048:2048 + TILES].rearrange("p (g j) -> p g j", j=J), AX.X,
                                         ALU.max))
            link(nc.vector.tensor_tensor(span[:, :], span[:, :], neg_base[:, :], ALU.add))
            link(nc.vector.tensor_reduce(widest[:, :], span[:, :], AX.X, ALU.max))
            link(nc.vector.tensor_scalar(passes_end[:, :], widest[0:1, :], 1.0, None, ALU.add))
            link(nc.vector.tensor_copy(p_iota, cst[:, C_IOTA:C_IOTA + J * WIN]))
            dve.wait_ge(s_mid, 1)
            dve.wait_ge(s_res1, 1)
            nc.vector.tensor_tensor(x_p[:, 2, :], x_res[:, :], x_p[:, 1, :], ALU.subtract).then_inc(s_parts, 1)
            dve.wait_ge(s_parts, 1)
            dve.wait_ge(s_set, 3)
            nc.vector.memset(widest[:, :], 0.0).then_inc(s_base, 1)
            end = dve.value_load(passes_end[0:1, 0:1], min_val=1, max_val=N)

            def static_below(g, n):
                return isinstance(g, int) and g < n

            def build_pick(g, v):
                dve.wait_ge(s_pd, g + 1)
                if not static_below(g, 2):
                    dve.wait_ge(s_px, g - 1)
                nc.vector.tensor_scalar(pick[:, v, :], p_dst, neg_base[0:K3, at(g)], node_off[0:K3, 0:1], ALU.add,
                                        ALU.is_equal).then_inc(s_pick, 1)

            def copy_x(g, v):
                dve.wait_ge(s_px, g + 1)
                if not static_below(g, 2):
                    dve.wait_ge(s_l1, g - 1)
                nc.vector.tensor_copy(xcat[0:2 * D, v, :], p_xc).then_inc(s_xc, 1)

            def add_sums(g):
                dve.wait_ge(s_agg, g + 1)
                if not static_below(g, 1):
                    dve.wait_ge(s_acc, g)
                first = dve.value_load(base_i[0:1, at(g)], min_val=0, max_val=N)
                win = sums[:, bass.ds(first, WIN)]
                nc.vector.tensor_tensor(win, win, p_agg, ALU.add).then_inc(s_acc, 1)

            def build_onehot(g, v):
                if not static_below(g, 2):
                    dve.wait_ge(s_agg, g - 1)
                nc.vector.tensor_tensor(onehot[:, v, :, :], p_iota.rearrange("p (j w) -> p j w", j=J),
                                        dst_rel[:, at(g), :].rearrange("p a j -> p (a j)").unsqueeze(2)
                                        .to_broadcast([P, J, WIN]), ALU.is_equal).then_inc(s_oh, 1)

            def step(s, u):
                static = isinstance(s, int)
                if not static or s < G:
                    copy_x(s, u % 2)
                if not static or s + R < G:
                    stage_indices(s + R, u)
                if not static or s >= 2:
                    add_sums(s - 2)
                if not static or s < G:
                    build_onehot(s, u % 2)
                if not static or s + 1 < G:
                    build_pick(s + 1, (u + 1) % 2)

            with dve.Fori(0, end, WIN) as off:
                build_pick(0, 0)
                for s in range(R):
                    step(s, s)
                with dve.Fori(1, LOOPS) as i:
                    for u in range(R):
                        step(i * R + u, u)
                for s in range(LOOPS * R, G + 2):
                    step(s, s % R)
                dve.wait_ge(s_acc, G)
                nc.vector.tensor_scalar(base_f[:, :], base_f[:, :], float(WIN), float(N), ALU.add, ALU.min).then_inc(s_acc, 1)
                dve.wait_ge(s_acc, G + 1)
                nc.vector.tensor_copy(base_i[:, :], base_f[:, :]).then_inc(s_acc, 1)
                nc.vector.tensor_scalar(node_off[:, :], node_off[:, :], float(WIN), None, ALU.add).then_inc(s_acc, 1)
                nc.vector.tensor_scalar(p_iota, p_iota, float(WIN), None, ALU.add).then_inc(s_acc, 1)
                dve.wait_ge(s_acc, G + 4)
                end_of_pass(dve, off)
                for g in range(R):
                    stage_indices(g, g)

            xv = x_nat[:, :].rearrange("p (c f) -> p c f", f=D)
            for n, (c0, w) in enumerate(CHUNKS):
                cs = slice(c0, c0 + w)
                prod = ps[0:NP, n, 0:w * (O + 1)].rearrange("p (c f) -> p c f", f=O + 1)
                dve.wait_ge(s_fin, n + 1)
                link(nc.vector.tensor_scalar(cnt[:, cs], prod[:, :, O], 1.0, None, ALU.max))
                link(nc.vector.reciprocal(rcnt[:, cs], cnt[:, cs]))
                link(nc.vector.tensor_tensor(z[:, cs, :], prod[:, :, 0:O], rcnt[:, cs].unsqueeze(2).to_broadcast([NP, w, O]),
                                             ALU.mult))
                link(nc.vector.tensor_tensor(z[:, cs, :], z[:, cs, :], xv[:, cs, :], ALU.add))
                link(nc.vector.tensor_reduce(mean[:, cs], z[:, cs, :], AX.X, ALU.add))
                nc.vector.tensor_scalar(mean[:, cs], mean[:, cs], 1.0 / O, None, ALU.mult).then_inc(s_z, 1)
                if n >= 1:
                    variance(dve, n - 1)
                if n >= 2:
                    inverse(dve, n - 2)
            variance(dve, len(CHUNKS) - 1)
            inverse(dve, len(CHUNKS) - 2)
            inverse(dve, len(CHUNKS) - 1)




_INS = ['x', 'src', 'dst', 'L0_gnn_W1', 'L0_gnn_b1', 'L0_gnn_W2', 'L0_gnn_b2', 'L0_gnn_W3', 'L0_gnn_b3', 'L0_gnn_W4',
        'L0_gnn_b4']


def kernel(**inputs):
    import numpy as _np
    import concourse.bacc as _bacc
    from concourse import mybir as _mybir
    from concourse.bass_utils import run_bass_kernel_spmd as _run

    nc = _bacc.Bacc("TRN2", target_bir_lowering=False, num_devices=1)
    arrays, args = {}, []
    for name in _INS:
        a = _np.ascontiguousarray(inputs[name])
        arrays[f"in_{name}"] = a
        args.append(nc.dram_tensor(f"in_{name}", a.shape, _mybir.dt.from_np(a.dtype), kind="ExternalInput").ap())
    c = _np.zeros((P, C_END), _np.float32)
    c[:, C_ID:C_ID + P] = _np.eye(P)
    c[:, C_IOTA:C_IOTA + J * WIN] = _np.tile(_np.arange(WIN), J)
    c[:, C_PMOD] = _np.arange(P) % WIN
    c[0:3, C_MASK:C_MASK + 3] = _np.eye(3)
    c[0, C_DIG:C_DIG + K3] = P
    c[1, C_DIG:C_DIG + K3] = 1
    arrays["in_consts"] = c
    args.append(nc.dram_tensor("in_consts", c.shape, _mybir.dt.from_np(c.dtype), kind="ExternalInput").ap())
    args.append(nc.dram_tensor("out_0", (N, O), F32, kind="ExternalOutput").ap())
    build(nc, *args)
    r = _run(nc, [arrays], core_ids=[0])
    return r.results[0]["out_0"]
```

```python
import concourse.bass as bass
from concourse import mybir
from contextlib import ExitStack

F32 = mybir.dt.float32
BF16 = mybir.dt.bfloat16
I32 = mybir.dt.int32
ALU = mybir.AluOpType
ACT = mybir.ActivationFunctionType
AX = mybir.AxisListType

N, E = 12500, 200000
D, H1, H2, H3 = 32, 64, 128, 64
O = 32
P = 128
EPS = 1e-5

T = P
J = 4
GE = J * T
G = -(-E // GE)
TILES = G * J
FULL = E // T
HALF = E - FULL * T
BLK = TILES // P
REST = TILES - BLK * P
WIN = P // 3
K3 = 3 * WIN
NPAD = N + WIN
R = 10
LOOPS = (G - R) // R
NP = 125
NC = N // NP
CH = 512 // (O + 1)
EDGE = (NC - 6 * CH) // 2
CHUNKS = [(0, EDGE)] + [(EDGE + CH * n, CH) for n in range(6)] + [(NC - EDGE, EDGE)]
LAG = 2
XH = 2
XQ = 4
ZERO1 = NPAD // 3
EARLY = 4

C_ID, C_IOTA, C_PMOD, C_MASK, C_END = 0, P, P + J * WIN, P + J * WIN + 1, P + J * WIN + 4


def build(nc, x, src, dst, W1, b1, W2, b2, W3, b3, W4, b4, consts, out):
    assert HALF * 2 == T and FULL == TILES - 2 and NP * NC == N
    ctx = ExitStack()
    with ctx:
        def sb(name, shape, dt):
            return ctx.enter_context(nc.sbuf_tensor(name, shape, dt))

        def sem(name):
            return ctx.enter_context(nc.semaphore(name))

        assert N < 2 ** 16
        x_parts = nc.dram_tensor("x_parts", (3, NPAD, D), BF16, kind="Internal").ap()
        dst_parts = nc.dram_tensor("dst_parts", (2, TILES * T), BF16, kind="Internal").ap()

        cst = sb("cst", [P, C_END], F32)
        ident = cst[:, C_ID:C_ID + P]
        ones2 = sb("ones2", [2, K3], BF16)
        zero = sb("zero", [O + 1, 1], F32)
        ones3 = sb("ones3", [3, P], BF16)
        node_off = sb("node_off", [P, 1], F32)
        w1cat = sb("w1cat", [P, P], F32)
        w1sub = sb("w1sub", [2 * D, H1], F32)
        w2s = sb("w2s", [P, H2], F32)
        w3s = sb("w3s", [H2, H3], F32)
        w4s = sb("w4s", [H3 + 1, O + 1], F32)
        w4mean = sb("w4mean", [H3 + 1, 1], F32)
        b1s = sb("b1s", [H1, 1], F32)
        b2s = sb("b2s", [H2, 1], F32)
        b3s = sb("b3s", [3, H3], F32)
        b3r = sb("b3r", [3, 2, H3], F32)
        b3p = sb("b3p", [3, 3, H3], BF16)
        b3m = sb("b3m", [3, J, H3], BF16)

        edge_i = sb("edge_i", [P, 2, BLK + 1, T], I32)
        src_i, dst_i = edge_i[:, 0, :, :], edge_i[:, 1, :, :]
        edge_f = sb("edge_f", [P, 2, BLK + 1, T], F32)
        src_f, dst_f = edge_f[:, 0, :, :], edge_f[:, 1, :, :]
        dst_b = sb("dst_b", [P, 2, BLK + 1, T], BF16)
        tile_min = sb("tile_min", [P, BLK + 1], F32)
        diag = sb("diag", [P, BLK + 1, T], F32)
        ones = sb("ones", [P, P], F32)
        src_t = sb("src_t", [P, TILES], I32)
        dst_rel = sb("dst_rel", [P, G, J], F32)
        neg_base = sb("neg_base", [P, G], F32)
        farthest = sb("farthest", [P, 1], F32)
        widest = sb("widest", [1, 1], F32)
        passes_end = sb("passes_end", [1, 1], I32)
        base_f = sb("base_f", [1, G], F32)
        base_i = sb("base_i", [1, G], I32)

        x_nat = sb("x_nat", [NP, NC * D], F32)
        x_res = sb("x_res", [NP, NC * D], F32)
        x_p = sb("x_p", [NP, 3, NC * D], BF16)
        zpad = sb("zpad", [WIN, 3, D], BF16)
        sums = sb("sums", [O + 1, NPAD], F32)

        idx = sb("idx", [P, R, J], I32)
        xj = sb("xj", [P, R, J, D], F32)
        xwin = sb("xwin", [K3, R, D], BF16)
        dstw = sb("dstw", [2, R, GE], BF16)
        pick = sb("pick", [K3, 2, GE], BF16)
        onehot = sb("onehot", [P, 2, J, WIN], F32)
        xcat = sb("xcat", [P, 2, GE], F32)
        h1 = sb("h1", [P, 2, GE], F32)
        h2 = sb("h2", [H2, 2, GE], F32)
        h3 = sb("h3", [P, 2, J, H3 + 1], F32)
        agg = sb("agg", [H3 + 1, 2, WIN], F32)

        def last(v):
            return v[:, 0:NC * O].rearrange("p (c f) -> p c f", f=O)

        cnt = sb("cnt", [NP, NC], F32)
        rcnt = sb("rcnt", [NP, NC], F32)
        xc = last(x_res[:, :])
        zc = last(edge_f[0:NP, :, :, :].rearrange("p a b e -> p (a b e)"))
        zq = last(edge_i[0:NP, :, :, :].rearrange("p a b e -> p (a b e)").bitcast(F32))
        xmean = sb("xmean", [NP, NC], F32)
        var = sb("var", [NP, NC], F32)
        std = sb("std", [NP, NC], F32)
        rstd = sb("rstd", [NP, NC], F32)
        eps = sb("eps", [NP, 1], F32)

        ps = ctx.enter_context(nc.psum_tensor("ps", [P, 8, 512], F32))
        psf = ps[:, :, :].rearrange("p b n -> p (b n)")
        p_dst = ps[0:K3, 0, :]
        p_xc = ps[0:2 * D, 1, :]
        p_h1 = ps[:, 2, :]
        p_h2 = ps[:, 3, :]
        p_h3 = ps[:, 4, 0:J * H3]
        p_agg = ps[0:H3 + 1, 5, 0:WIN]
        p_iota = ps[:, 6, 0:J * WIN]
        p_msg = ps[0:O + 1, 7, 0:WIN]
        p_lo, p_hi = psf[:, 0:TILES], psf[:, 2048:2048 + TILES]
        p_far = ps[0:1, 0, 0:P]

        s_first = [sem(f"first_indices_in{n}") for n in range(EARLY // 2)]
        s_src, s_dst, s_cst = sem("src_in"), sem("dst_in"), sem("cst_in")
        s_x, s_w = sem("x_in"), sem("weights_in")
        s_srcf, s_dstf = sem("src_as_float"), sem("dst_as_float")
        s_srcT, s_dstT, s_idx = sem("src_transposed"), sem("dst_transposed"), sem("indices")
        s_diag, s_minb, s_far, s_farT = sem("diagonals"), sem("minima_spread"), sem("farthest"), sem("farthest_as_row")
        s_base, s_end = sem("bases"), sem("number_of_passes")
        s_dhi, s_dlo, s_dst_st = sem("dst_part0"), sem("dst_part1"), sem("dst_parts_stored")
        s_hi, s_mid, s_lo, s_xst = sem("x_part0"), sem("x_part1"), sem("x_part2"), sem("x_parts_stored")
        s_res = sem("x_minus_part0")
        s_ones, s_zero, s_wz, s_set, s_w4z = (sem("ones_set"), sem("zero_set"), sem("zero_rows_set"), sem("pads_set"),
                                              sem("w4_zeroed"))
        s_sum0, s_ready = sem("sums_zeroed"), sem("weights_ready")
        s_vc = sem("vector_chain")
        s_fin, s_m, s_z, s_sq, s_var, s_std, s_rstd, s_y, s_out = (
            sem("sums_transposed"), sem("mean_message"), sem("z_ready"), sem("z_squared"), sem("var_ready"),
            sem("std_ready"),
            sem("rstd_ready"), sem("y_ready"), sem("out_stored"))

        s_gath = [sem(f"gathered{u}") for u in range(R)]
        s_xwin = [sem(f"window_in{u}") for u in range(R)]
        s_dwin = [sem(f"dst_row_in{u}") for u in range(R)]
        s_pd, s_px, s_l1, s_l2, s_l3, s_agg, s_msg = (sem("dst_spread"), sem("x_in_psum"), sem("layer1"), sem("layer2"),
                                                      sem("layer3"), sem("window_summed"), sem("messages"))
        s_stage = sem("indices_staged")
        s_stage0 = sem("first_groups_staged")
        s_begun = sem("gathers_begun")
        s_pick, s_oh, s_xc, s_copied, s_acc = (sem("pick_built"), sem("onehot_built"), sem("x_copied"),
                                               sem("window_sums_copied"), sem("sums_added"))
        s_moved, s_centre = sem("windows_moved"), sem("centring_chain")
        s_r1, s_r2, s_r3 = sem("relu1"), sem("relu2"), sem("relu3")
        s_arrive = sem("pass_arrived")
        per_pass = range(s_gath[0].num, s_arrive.num + 1)
        s_open = sem("pass_open")

        block = ctx.enter_context(nc.Block())

        def rows_of(v):
            return (v[0:BLK * P * T].rearrange("(b p e) -> p b e", p=P, e=T),
                    v[BLK * P * T:FULL * T].rearrange("(p e) -> p e", e=T))

        def piece(h):
            return slice(h * NC * D // XH, (h + 1) * NC * D // XH)

        def end_of_pass(eng, off):
            eng.sem_inc(s_arrive, 1)
            eng.wait_ge(s_open, off + WIN)

        def add_x(pool, n):
            c0, w = CHUNKS[n]
            at = slice(c0, c0 + w)
            pool.wait_ge(s_m, n + 1)
            nc.gpsimd.tensor_tensor(zc[:, at, :], zc[:, at, :], xc[:, at, :], ALU.add).then_inc(s_z, 1)

        def normalise(pool, n):
            c0, w = CHUNKS[n]
            at = slice(c0, c0 + w)
            pool.wait_ge(s_rstd, n + 1)
            nc.gpsimd.tensor_tensor(zc[:, at, :], zc[:, at, :], rstd[:, at].unsqueeze(2).to_broadcast([NP, w, O]),
                                    ALU.mult).then_inc(s_y, 1)

        def root(act, n):
            c0, w = CHUNKS[n]
            act.wait_ge(s_var, n + 1)
            nc.scalar.activation(std[:, c0:c0 + w], var[:, c0:c0 + w], ACT.Sqrt, bias=eps[:, 0:1],
                                 scale=1.0 / O).then_inc(s_std, 1)

        def variance(dve, n):
            c0, w = CHUNKS[n]
            dve.wait_ge(s_sq, n + 1)
            nc.vector.tensor_reduce(var[:, c0:c0 + w], zq[:, c0:c0 + w, :], AX.X, ALU.add).then_inc(s_var, 1)

        def inverse(dve, n):
            c0, w = CHUNKS[n]
            dve.wait_ge(s_std, n + 1)
            nc.vector.reciprocal(rstd[:, c0:c0 + w], std[:, c0:c0 + w]).then_inc(s_rstd, 1)

        @block.sync
        def _(sp):
            def load_edges(v, t, s):
                full, rest = rows_of(v)
                sp.dma_start(t[:, 0:BLK, :], full).then_inc(s, 16)
                sp.dma_start(t[0:REST - 2, BLK, :], rest).then_inc(s, 16)
                sp.dma_start(t[REST - 2:REST, BLK, :].rearrange("p (h e) -> p h e", e=HALF),
                             v[FULL * T:E].unsqueeze(0).unsqueeze(0).to_broadcast([2, 2, HALF])).then_inc(s, 16)

            with nc.allow_non_contiguous_dma("four-byte runs, of a few groups only"):
                for g in range(0, EARLY, 2):
                    sp.dma_start(idx[:, g:g + 2, :],
                                 src[g * GE:(g + 2) * GE].rearrange("(g j e) -> e g j", j=J, e=T))\
                        .then_inc(s_first[g // 2], 16)
            load_edges(dst, dst_i, s_dst)
            load_edges(src, src_i, s_src)
            sp.dma_start(x_nat[:, :], x.rearrange("(p c) f -> p (c f)", p=NP)).then_inc(s_x, 16)
            sp.wait_ge(s_wz, 1)
            sp.dma_start(w1cat[0:D, 0:H1], W1[D:2 * D, :]).then_inc(s_w, 16)
            sp.dma_start(w1cat[D:2 * D, 0:H1], W1[0:D, :]).then_inc(s_w, 16)
            sp.dma_start(w1sub[D:2 * D, :], W1[D:2 * D, :]).then_inc(s_w, 16)
            sp.dma_start(w2s[0:H1, :], W2).then_inc(s_w, 16)
            sp.dma_start(w3s[:, :], W3).then_inc(s_w, 16)
            sp.dma_start(b1s[:, :], b1.rearrange("(n a) -> n a", a=1)).then_inc(s_w, 16)
            sp.dma_start(b2s[:, :], b2.rearrange("(n a) -> n a", a=1)).then_inc(s_w, 16)
            sp.dma_start(b3s[:, :], b3.unsqueeze(0).to_broadcast([3, H3])).then_inc(s_w, 16)
            sp.wait_ge(s_w4z, 2)
            sp.dma_start(w4s[0:H3, 0:O], W4).then_inc(s_w, 16)
            sp.dma_start(w4s[H3:H3 + 1, 0:O], b4.rearrange("(a n) -> a n", a=1)).then_inc(s_w, 16)
            sp.wait_ge(s_dhi, 2)
            sp.wait_ge(s_dlo, 2)
            for k in range(2):
                row = dst_parts[k, :]
                sp.dma_start(row[0:BLK * P * T].rearrange("(b p e) -> p b e", p=P, e=T),
                             dst_b[:, k, 0:BLK, :]).then_inc(s_dst_st, 16)
                sp.dma_start(row[BLK * P * T:TILES * T].rearrange("(p e) -> p e", e=T),
                             dst_b[0:REST, k, BLK, :]).then_inc(s_dst_st, 16)
            sp.wait_ge(s_set, 1)
            sp.dma_start(x_parts[:, N:NPAD, :].rearrange("k n f -> n k f"), zpad[:, :, :]).then_inc(s_xst, 16)
            for k, s in enumerate((s_hi, s_mid, s_lo)):
                for h in range(XH):
                    sp.wait_ge(s, h + 1)
                    sp.dma_start(x_parts[k, 0:N, :].rearrange("(p c) f -> p (c f)", p=NP)[:, piece(h)],
                                 x_p[:, k, piece(h)]).then_inc(s_xst, 16)
            sp.wait_ge(s_dst_st, 4 * 16)
            sp.wait_ge(s_xst, (3 * XH + 1) * 16)
            sp.wait_ge(s_base, 1)

            def load(g, u):
                if not (isinstance(g, int) and g < R):
                    sp.wait_ge(s_px, g - R + 1)
                col = g if isinstance(g, int) else bass.ds(g, 1)
                col = base_i[0:1, g:g + 1] if isinstance(g, int) else base_i[0:1, col]
                first = sp.value_load(col, min_val=0, max_val=N)
                sp.dma_start(xwin[:, u, :], x_parts[:, bass.ds(first, WIN), :]).then_inc(s_xwin[u], 16)
                at = slice(g * GE, (g + 1) * GE) if isinstance(g, int) else bass.ds(g * GE, GE)
                sp.dma_start(dstw[:, u, :], dst_parts[:, at]).then_inc(s_dwin[u], 16)

            for g in range(R):
                load(g, g)
            sp.wait_ge(s_end, 1)
            end = sp.value_load(passes_end[0:1, 0:1], min_val=1, max_val=N)
            with sp.Fori(0, end, WIN) as off:
                with sp.Fori(1, LOOPS) as i:
                    for u in range(R):
                        load(i * R + u, u)
                for g in range(LOOPS * R, G):
                    load(g, g % R)
                sp.wait_ge(s_acc, G)
                sp.wait_ge(s_arrive, 4)
                sp.sem_clear(per_pass)
                sp.sem_inc(s_open, WIN)
                with sp.If(off + WIN < end):
                    for g in range(R):
                        load(g, g)

            for n, (c0, w) in enumerate(CHUNKS):
                sp.wait_ge(s_y, n + 1)
                sp.dma_start(out.rearrange("(p c) f -> p c f", p=NP)[:, c0:c0 + w, :], zc[:, c0:c0 + w, :])\
                    .then_inc(s_out, 16)
            sp.wait_ge(s_out, 16 * len(CHUNKS))

        @block.gpsimd
        def _(pool):
            nc.gpsimd.memset(zpad[:, :, :], 0.0).then_inc(s_set, 1)
            nc.gpsimd.memset(w4s[:, :], 0.0).then_inc(s_w4z, 1)
            pool.wait_ge(s_w4z, 1)
            nc.gpsimd.memset(w4s[H3:H3 + 1, O:O + 1], 1.0).then_inc(s_w4z, 1)

            def gather(g, u):
                for j in range(J):
                    if isinstance(g, int) and g * J + j == TILES - 1:
                        break
                    pool.indirect_dma_start(out=xj[:, u, j, :], out_offset=None, in_=x,
                                            in_offset=bass.IndirectOffsetOnAxis(ap=idx[:, u, j:j + 1], axis=0))\
                        .then_inc(s_gath[u], 16)

            def gather_turn(i, groups):
                for u in range(groups):
                    if u % 2 == 0:
                        pool.wait_ge(s_stage, i * (R // 2) + u // 2 + 1 - EARLY // 2)
                        if not isinstance(i, int):
                            pool.sem_inc(s_begun, 1)
                    gather(i * R + u, u)

            def gather_first(early):
                for g in range(R):
                    if g < EARLY and g % 2 == 0:
                        early(g)
                    if g >= EARLY and g % 2 == 0:
                        pool.wait_ge(s_stage, (g - EARLY) // 2 + 1)
                    gather(g, g)

            gather_first(lambda g: pool.wait_ge(s_first[g // 2], 16))
            pool.wait_ge(s_end, 1)
            end = pool.value_load(passes_end[0:1, 0:1], min_val=1, max_val=N)
            with pool.Fori(0, end, WIN) as off:
                with pool.Fori(1, LOOPS) as i:
                    gather_turn(i, R)
                for i in range(LOOPS, -(-G // R)):
                    gather_turn(i, min(R, G - i * R))
                for u in range(R):
                    pool.wait_ge(s_gath[u], 16 * sum(1 for t in range(TILES - 1) if t // J % R == u))
                pool.dma_reset(range(s_gath[0].num, s_gath[-1].num + 1))
                end_of_pass(pool, off)
                pool.sem_inc(s_begun, 1)
                with pool.If(off + WIN < end):
                    gather_first(lambda g: pool.wait_ge(s_stage0, g // 2 + 1))

            for n in range(len(CHUNKS)):
                add_x(pool, n)
                if n >= LAG:
                    normalise(pool, n - LAG)
            for n in range(len(CHUNKS) - LAG, len(CHUNKS)):
                normalise(pool, n)

        @block.scalar
        def _(act):
            act.dma_start(cst[:, :], consts).then_inc(s_cst, 16)
            act.wait_ge(s_zero, 1)
            nc.scalar.activation(sums[:, 0:ZERO1], zero[:, 0:1].to_broadcast([O + 1, ZERO1]), ACT.Copy)
            act.wait_ge(s_dst, 3 * 16)
            nc.scalar.activation(dst_b[:, 0, 0:BLK, :], dst_i[:, 0:BLK, :], ACT.Copy).then_inc(s_dhi, 1)
            nc.scalar.activation(dst_b[0:REST, 0, BLK, :], dst_i[0:REST, BLK, :], ACT.Copy).then_inc(s_dhi, 1)
            act.wait_ge(s_src, 3 * 16)
            nc.scalar.activation(src_f[:, 0:BLK, :], src_i[:, 0:BLK, :], ACT.Copy).then_inc(s_srcf, 1)
            nc.scalar.activation(src_f[0:REST, BLK, :], src_i[0:REST, BLK, :], ACT.Copy).then_inc(s_srcf, 1)
            act.wait_ge(s_x, 16)
            for h in range(XH):
                nc.scalar.activation(x_p[:, 0, piece(h)], x_nat[:, piece(h)], ACT.Copy).then_inc(s_hi, 1)
            for h in range(XH):
                act.wait_ge(s_res, h + 1)
                nc.scalar.activation(x_p[:, 1, piece(h)], x_res[:, piece(h)], ACT.Copy).then_inc(s_mid, 1)
            nc.scalar.activation(sums[:, ZERO1:NPAD], zero[:, 0:1].to_broadcast([O + 1, NPAD - ZERO1]),
                                 ACT.Copy).then_inc(s_sum0, 1)
            act.wait_ge(s_w, 10 * 16)
            act.wait_ge(s_set, 2)
            act.wait_ge(s_end, 1)
            end = act.value_load(passes_end[0:1, 0:1], min_val=1, max_val=N)

            def static_below(g, n):
                return isinstance(g, int) and g < n

            def relu1(g, v):
                act.wait_ge(s_l1, g + 1)
                if not static_below(g, 2):
                    act.wait_ge(s_l2, g - 1)
                nc.scalar.activation(h1[0:H1, v, :], p_h1[0:H1, :], ACT.Relu, bias=b1s[:, 0:1]).then_inc(s_r1, 1)

            def relu2(g, v):
                act.wait_ge(s_l2, g + 1)
                if not static_below(g, 2):
                    act.wait_ge(s_l3, g - 1)
                nc.scalar.activation(h2[:, v, :], p_h2, ACT.Relu, bias=b2s[:, 0:1]).then_inc(s_r2, 1)

            def relu3(g, v):
                act.wait_ge(s_l3, g + 1)
                if not static_below(g, 2):
                    act.wait_ge(s_agg, g - 1)
                nc.scalar.activation(h3[:, v, :, 0:H3], p_h3.rearrange("p (j f) -> p j f", j=J),
                                     ACT.Relu).then_inc(s_r3, 1)

            def step(s, u, last=False):
                first = isinstance(s, int) and s == 0
                if not first:
                    relu2(s - 1, (u - 1) % 2)
                if not last:
                    relu1(s, u % 2)
                if not first:
                    relu3(s - 1, (u - 1) % 2)

            with act.Fori(0, end, WIN) as off:
                for s in range(R):
                    step(s, s)
                with act.Fori(1, LOOPS) as i:
                    for u in range(R):
                        step(i * R + u, u)
                for s in range(LOOPS * R, G + 1):
                    step(s, s % R, last=s == G)
                end_of_pass(act, off)

            nc.scalar.activation(std[:, 0:1], eps[:, 0:1], ACT.Sqrt)
            for n, (c0, w) in enumerate(CHUNKS):
                at = slice(c0, c0 + w)
                act.wait_ge(s_z, n + 1)
                nc.scalar.activation(zq[:, at, :], zc[:, at, :], ACT.Square).then_inc(s_sq, 1)
                if n >= 1:
                    root(act, n - 1)
            root(act, len(CHUNKS) - 1)


        @block.tensor
        def _(pe):
            pe.wait_ge(s_cst, 16)
            for v, bank, ready, done in ((dst_f, 4, s_dstf, s_dstT), (src_f, 0, s_srcf, s_srcT)):
                pe.wait_ge(ready, 2)
                for b in range(BLK + 1):
                    k = P if b < BLK else REST
                    nc.tensor.transpose(ps[:, bank + b // 4, b % 4 * P:b % 4 * P + k], v[0:k, b, :], ident[0:k, 0:k])\
                        .then_inc(done, 1)
            pe.wait_ge(s_ones, 1)
            pe.wait_ge(s_diag, 2)
            pe.wait_ge(s_idx, 1)
            for b in range(BLK + 1):
                k = P if b < BLK else REST
                nc.tensor.matmul(ps[:, b // 4, b % 4 * P:b % 4 * P + k], ones[0:k, :], diag[0:k, b, 0:k],
                                 start=True, stop=True).then_inc(s_minb, 1)
            pe.wait_ge(s_far, 1)
            nc.tensor.transpose(p_far, farthest[:, :], ident).then_inc(s_farT, 1)
            pe.wait_ge(s_end, 1)
            end = pe.value_load(passes_end[0:1, 0:1], min_val=1, max_val=N)
            pe.wait_ge(s_ready, 1)

            def static_below(g, n):
                return isinstance(g, int) and g < n

            def spread_dst(g, u, i):
                pe.wait_ge(s_dwin[u], 16 * (i + 1))
                if not static_below(g, 1):
                    pe.wait_ge(s_pick, g)
                nc.tensor.matmul(p_dst, ones2[:, :], dstw[:, u, :], start=True, stop=True).then_inc(s_pd, 1)

            def collect_x(g, u, i, v):
                pe.wait_ge(s_gath[u], 16 * J * (i + 1) - (16 if isinstance(g, int) and g == G - 1 else 0))
                pe.wait_ge(s_xwin[u], 16 * (i + 1))
                pe.wait_ge(s_pick, g + 1)
                if not static_below(g, 1):
                    pe.wait_ge(s_xc, g)
                for j in range(J):
                    nc.tensor.transpose(p_xc[0:D, j * T:(j + 1) * T], xj[:, u, j, :], ident)
                nc.tensor.matmul(p_xc[D:2 * D, :], xwin[:, u, :], pick[:, v, :], start=True, stop=True).then_inc(s_px, 1)

            def layer1(g, v):
                pe.wait_ge(s_xc, g + 1)
                if not static_below(g, 1):
                    pe.wait_ge(s_r1, g)
                nc.tensor.matmul(p_h1, w1cat[:, :], xcat[:, v, :], start=True, stop=True).then_inc(s_l1, 1)

            def layer2(g, v):
                pe.wait_ge(s_r1, g + 1)
                if not static_below(g, 1):
                    pe.wait_ge(s_r2, g)
                nc.tensor.matmul(p_h2, w2s[:, :], h1[:, v, :], start=True, stop=True).then_inc(s_l2, 1)

            def layer3(g, v):
                pe.wait_ge(s_r2, g + 1)
                if not static_below(g, 1):
                    pe.wait_ge(s_r3, g)
                nc.tensor.matmul(p_h3, ones3[:, :], b3m[:, :, :].rearrange("p j f -> p (j f)"), start=True, stop=False)
                for j in range(J):
                    last = nc.tensor.matmul(p_h3[:, j * H3:(j + 1) * H3], h2[:, v, j * T:(j + 1) * T], w3s[:, :],
                                            start=False, stop=j == J - 1)
                last.then_inc(s_l3, 1)

            def sum_window(g, v):
                pe.wait_ge(s_r3, g + 1)
                pe.wait_ge(s_oh, g + 1)
                if not static_below(g, 1):
                    pe.wait_ge(s_copied, g)
                for j in range(J):
                    last = nc.tensor.matmul(p_agg, h3[:, v, j, :], onehot[:, v, j, :], start=j == 0, stop=j == J - 1)
                last.then_inc(s_agg, 1)

            def message(g, v):
                pe.wait_ge(s_copied, g + 1)
                if not static_below(g, 1):
                    pe.wait_ge(s_acc, g)
                nc.tensor.matmul(p_msg, w4s[:, :], agg[:, v, :], start=True, stop=True).then_inc(s_msg, 1)

            def step(s, i, u):
                static = isinstance(s, int)
                if not static or s < G:
                    collect_x(s, u, i, u % 2)
                if not static or s + 1 < G:
                    spread_dst(s + 1, (u + 1) % R, i + (u + 1) // R)
                if not static or s >= 3:
                    message(s - 3, (u + 1) % 2)
                if not static or 1 <= s <= G:
                    layer2(s - 1, (u - 1) % 2)
                if not static or s < G:
                    layer1(s, u % 2)
                if not static or 2 <= s <= G + 1:
                    sum_window(s - 2, u % 2)
                if not static or 1 <= s <= G:
                    layer3(s - 1, (u - 1) % 2)

            with pe.Fori(0, end, WIN) as off:
                spread_dst(0, 0, 0)
                for s in range(R):
                    step(s, 0, s)
                with pe.Fori(1, LOOPS) as i:
                    for u in range(R):
                        step(i * R + u, i, u)
                for s in range(LOOPS * R, G + 3):
                    step(s, s // R, s % R)
                end_of_pass(pe, off)

            for n, (c0, w) in enumerate(CHUNKS):
                for c in range(w):
                    last = nc.tensor.transpose(ps[0:NP, n, c * (O + 1):(c + 1) * (O + 1)],
                                               sums[:, c0 + c:N:NC], ident[0:O + 1, 0:O + 1])
                last.then_inc(s_fin, 1)

        @block.vector
        def _(dve):
            chain = [0]

            def at(g):
                return slice(g, g + 1) if isinstance(g, int) else bass.ds(g, 1)

            def stage_pair(g, u, s):
                w = min(2 * J, TILES - g * J) if isinstance(g, int) else 2 * J
                nc.vector.tensor_copy(idx[:, :, :].rearrange("p a j -> p (a j)")[:, u * J:u * J + w],
                                      src_t[:, bass.ds(g * J, w)]).then_inc(s, 1)

            def link(ins):
                chain[0] += 1
                ins.then_inc(s_vc, 1)
                dve.wait_ge(s_vc, chain[0])

            nc.vector.memset(zero[:, :], 0.0).then_inc(s_zero, 1)
            nc.vector.memset(w1cat[:, :], 0.0).then_inc(s_wz, 1)
            nc.vector.memset(ones[:, :], 1.0).then_inc(s_ones, 1)
            nc.vector.memset(h3[:, :, :, :], 1.0).then_inc(s_set, 1)
            nc.vector.memset(w2s[H1:P, :], 0.0)
            nc.vector.memset(ones2[:, :], 1.0)
            nc.vector.memset(ones3[:, :], 1.0)
            nc.vector.memset(eps[:, :], EPS).then_inc(s_set, 1)
            nc.vector.memset(xcat[2 * D:P, :, :], 0.0)
            nc.vector.memset(h1[H1:P, :, :], 0.0)
            dve.wait_ge(s_dst, 3 * 16)
            nc.vector.tensor_copy(dst_f[:, 0:BLK, :], dst_i[:, 0:BLK, :]).then_inc(s_dstf, 1)
            nc.vector.tensor_copy(dst_f[0:REST, BLK, :], dst_i[0:REST, BLK, :]).then_inc(s_dstf, 1)
            dve.wait_ge(s_dstf, 2)
            nc.vector.tensor_reduce(tile_min[:, 0:BLK], dst_f[:, 0:BLK, :], AX.X, ALU.min)
            link(nc.vector.tensor_reduce(tile_min[0:REST, BLK:BLK + 1], dst_f[0:REST, BLK, :], AX.X, ALU.min))
            dve.wait_ge(s_cst, 16)
            nc.vector.tensor_tensor(diag[:, 0:BLK, :], ident.unsqueeze(1).to_broadcast([P, BLK, P]),
                                    tile_min[:, 0:BLK].unsqueeze(2).to_broadcast([P, BLK, P]), ALU.mult).then_inc(s_diag, 1)
            nc.vector.tensor_scalar(diag[0:REST, BLK, :], ident[0:REST, :], tile_min[0:REST, BLK:BLK + 1], None,
                                    ALU.mult).then_inc(s_diag, 1)
            nc.vector.tensor_copy(node_off[:, :], cst[:, C_PMOD:C_PMOD + 1])
            dve.wait_ge(s_dhi, 2)
            nc.vector.tensor_tensor(dst_b[:, 1, 0:BLK, :], dst_f[:, 0:BLK, :], dst_b[:, 0, 0:BLK, :],
                                    ALU.subtract).then_inc(s_dlo, 1)
            nc.vector.tensor_tensor(dst_b[0:REST, 1, BLK, :], dst_f[0:REST, BLK, :], dst_b[0:REST, 0, BLK, :],
                                    ALU.subtract).then_inc(s_dlo, 1)
            dve.wait_ge(s_srcT, BLK + 1)
            nc.vector.tensor_copy(src_t[:, :], p_lo).then_inc(s_idx, 1)
            dve.wait_ge(s_idx, 1)
            for g in range(EARLY, R, 2):
                stage_pair(g, g, s_stage)
            for h in range(XH):
                dve.wait_ge(s_hi, h + 1)
                nc.vector.tensor_tensor(x_res[:, piece(h)], x_nat[:, piece(h)], x_p[:, 0, piece(h)],
                                        ALU.subtract).then_inc(s_res, 1)
            for h in range(XH):
                dve.wait_ge(s_mid, h + 1)
                nc.vector.tensor_tensor(x_p[:, 2, piece(h)], x_res[:, piece(h)], x_p[:, 1, piece(h)],
                                        ALU.subtract).then_inc(s_lo, 1)
            dve.wait_ge(s_minb, BLK + 1)
            link(nc.vector.tensor_reduce(neg_base[:, :], p_lo.rearrange("p (g j) -> p g j", j=J), AX.X,
                                         ALU.min, negate=True))
            link(nc.vector.tensor_scalar(base_f[:, :], neg_base[0:1, :], -1.0, None, ALU.mult))
            nc.vector.tensor_copy(base_i[:, :], base_f[:, :]).then_inc(s_base, 1)
            dve.wait_ge(s_dstT, BLK + 1)
            link(nc.vector.tensor_tensor(dst_rel[:, :, :], p_hi.rearrange("p (g j) -> p g j", j=J),
                                         neg_base[:, :].unsqueeze(2).to_broadcast([P, G, J]), ALU.add))
            nc.vector.tensor_reduce(farthest[:, :], dst_rel[:, :, :].rearrange("p g j -> p (g j)"), AX.X,
                                    ALU.max).then_inc(s_far, 1)
            dve.wait_ge(s_far, 1)
            nc.vector.memset(dst_rel[HALF:P, G - 1, J - 2:J - 1], -1.0)
            nc.vector.memset(dst_rel[:, G - 1, J - 1:J], -1.0)
            nc.vector.tensor_copy(p_iota, cst[:, C_IOTA:C_IOTA + J * WIN])
            dve.wait_ge(s_w, 10 * 16)
            nc.vector.tensor_tensor(w1cat[D:2 * D, 0:H1], w1cat[D:2 * D, 0:H1], w1sub[D:2 * D, :], ALU.subtract)
            nc.vector.tensor_reduce(w4mean[:, :], w4s[:, 0:O], AX.X, ALU.add)
            link(nc.vector.tensor_copy(b3p[:, 0, :], b3s[:, :]))
            dve.wait_ge(s_farT, 1)
            nc.vector.tensor_reduce(widest[:, :], p_far, AX.X, ALU.max)
            nc.vector.tensor_scalar(w4mean[:, :], w4mean[:, :], -1.0 / O, None, ALU.mult)
            link(nc.vector.tensor_tensor(b3r[:, 0, :], b3s[:, :], b3p[:, 0, :], ALU.subtract))
            nc.vector.tensor_scalar(passes_end[:, :], widest[:, :], 1.0, None, ALU.add).then_inc(s_end, 1)
            nc.vector.tensor_scalar(w4s[:, 0:O], w4s[:, 0:O], w4mean[:, 0:1], None, ALU.add)
            link(nc.vector.tensor_copy(b3p[:, 1, :], b3r[:, 0, :]))
            link(nc.vector.tensor_tensor(b3p[:, 2, :], b3r[:, 0, :], b3p[:, 1, :], ALU.subtract))
            link(nc.vector.tensor_scalar(b3r[:, 0, :], b3p[:, 0, :], cst[0:3, C_MASK:C_MASK + 1], None, ALU.mult))
            link(nc.vector.scalar_tensor_tensor(b3r[:, 1, :], b3p[:, 1, :], cst[0:3, C_MASK + 1:C_MASK + 2], b3r[:, 0, :],
                                                ALU.mult, ALU.add))
            link(nc.vector.scalar_tensor_tensor(b3r[:, 0, :], b3p[:, 2, :], cst[0:3, C_MASK + 2:C_MASK + 3], b3r[:, 1, :],
                                                ALU.mult, ALU.add))
            nc.vector.tensor_copy(b3m[:, :, :], b3r[:, 0:1, :].to_broadcast([3, J, H3])).then_inc(s_ready, 1)
            dve.wait_ge(s_end, 1)
            end = dve.value_load(passes_end[0:1, 0:1], min_val=1, max_val=N)

            linked = [0]

            def link_pass(ins):
                linked[0] += 1
                ins.then_inc(s_centre, 1)
                dve.wait_ge(s_centre, linked[0])

            def static_below(g, n):
                return isinstance(g, int) and g < n

            def build_pick(g, v):
                dve.wait_ge(s_pd, g + 1)
                if not static_below(g, 2):
                    dve.wait_ge(s_px, g - 1)
                nc.vector.tensor_scalar(pick[:, v, :], p_dst, neg_base[0:K3, at(g)], node_off[0:K3, 0:1], ALU.add,
                                        ALU.is_equal).then_inc(s_pick, 1)

            def copy_x(g, v):
                dve.wait_ge(s_px, g + 1)
                if not static_below(g, 2):
                    dve.wait_ge(s_l1, g - 1)
                nc.vector.tensor_copy(xcat[0:2 * D, v, :], p_xc).then_inc(s_xc, 1)

            def copy_sums(g, v):
                dve.wait_ge(s_agg, g + 1)
                if not static_below(g, 2):
                    dve.wait_ge(s_msg, g - 1)
                nc.vector.tensor_copy(agg[:, v, :], p_agg).then_inc(s_copied, 1)

            def add_messages(g):
                dve.wait_ge(s_msg, g + 1)
                if static_below(g, 1):
                    dve.wait_ge(s_sum0, 1)
                else:
                    dve.wait_ge(s_acc, g)
                first = dve.value_load(base_i[0:1, at(g)], min_val=0, max_val=N)
                win = sums[:, bass.ds(first, WIN)]
                nc.vector.tensor_tensor(win, win, p_msg, ALU.add).then_inc(s_acc, 1)

            def build_onehot(g, v):
                if not static_below(g, 2):
                    dve.wait_ge(s_agg, g - 1)
                nc.vector.tensor_tensor(onehot[:, v, :, :], p_iota.rearrange("p (j w) -> p j w", j=J),
                                        dst_rel[:, at(g), :].rearrange("p a j -> p (a j)").unsqueeze(2)
                                        .to_broadcast([P, J, WIN]), ALU.is_equal).then_inc(s_oh, 1)

            def centre_x(q):
                cs = slice(q * NC // XQ, (q + 1) * NC // XQ)
                xv = x_nat[:, :].rearrange("p (c f) -> p c f", f=D)[:, cs, :]
                link_pass(nc.vector.tensor_reduce(xmean[:, cs], xv, AX.X, ALU.add))
                link_pass(nc.vector.tensor_scalar(xmean[:, cs], xmean[:, cs], 1.0 / D, None, ALU.mult))
                nc.vector.tensor_tensor(xc[:, cs, :], xv, xmean[:, cs].unsqueeze(2).to_broadcast([NP, NC // XQ, D]),
                                        ALU.subtract)

            def step(s, u):
                static = isinstance(s, int)
                if not static or s < G:
                    copy_x(s, u % 2)
                if not static or s + 1 < G:
                    build_pick(s + 1, (u + 1) % 2)
                if u % 2 and (not static or s + R - 1 < G):
                    stage_pair(s + R - 1, u - 1, s_stage)
                if not static or s >= 3:
                    add_messages(s - 3)
                if not static or 2 <= s <= G + 1:
                    copy_sums(s - 2, u % 2)
                if not static or s < G:
                    build_onehot(s, u % 2)

            with dve.Fori(0, end, WIN) as off:
                build_pick(0, 0)
                for s in range(R):
                    step(s, s)
                with dve.Fori(1, LOOPS) as i:
                    for u in range(R):
                        step(i * R + u, u)
                for s in range(LOOPS * R, G + 3):
                    step(s, s % R)
                    if s < LOOPS * R + XQ:
                        centre_x(s - LOOPS * R)
                    if s == G - 1:
                        nc.vector.tensor_scalar(base_f[:, :], base_f[:, :], float(WIN), float(N), ALU.add,
                                                ALU.min).then_inc(s_moved, 1)
                        nc.vector.tensor_scalar(node_off[:, :], node_off[:, :], float(WIN), None,
                                                ALU.add).then_inc(s_moved, 1)
                        nc.vector.tensor_scalar(p_iota, p_iota, float(WIN), None, ALU.add).then_inc(s_moved, 1)
                dve.wait_ge(s_acc, G)
                dve.wait_ge(s_moved, 3)
                nc.vector.tensor_copy(base_i[:, :], base_f[:, :]).then_inc(s_moved, 1)
                dve.wait_ge(s_moved, 4)
                end_of_pass(dve, off)
                for g in range(0, EARLY, 2):
                    stage_pair(g, g, s_stage0)
                for g in range(EARLY, R, 2):
                    stage_pair(g, g, s_stage)

            for n in range(len(CHUNKS) + LAG + 1):
                if n > LAG:
                    variance(dve, n - LAG - 1)
                if n < len(CHUNKS):
                    c0, w = CHUNKS[n]
                    cs = slice(c0, c0 + w)
                    prod = ps[0:NP, n, 0:w * (O + 1)].rearrange("p (c f) -> p c f", f=O + 1)
                    dve.wait_ge(s_fin, n + 1)
                    link(nc.vector.tensor_scalar(cnt[:, cs], prod[:, :, O], 1.0, None, ALU.max))
                    link(nc.vector.reciprocal(rcnt[:, cs], cnt[:, cs]))
                    nc.vector.tensor_tensor(zc[:, cs, :], prod[:, :, 0:O],
                                            rcnt[:, cs].unsqueeze(2).to_broadcast([NP, w, O]), ALU.mult).then_inc(s_m, 1)
                if n > LAG:
                    inverse(dve, n - LAG - 1)


_INS = ['x', 'src', 'dst', 'L0_gnn_W1', 'L0_gnn_b1', 'L0_gnn_W2', 'L0_gnn_b2', 'L0_gnn_W3', 'L0_gnn_b3', 'L0_gnn_W4',
        'L0_gnn_b4']


def kernel(**inputs):
    import numpy as _np
    import concourse.bacc as _bacc
    from concourse import mybir as _mybir
    from concourse.bass_utils import run_bass_kernel_spmd as _run

    nc = _bacc.Bacc("TRN2", target_bir_lowering=False, num_devices=1)
    arrays, args = {}, []
    for name in _INS:
        a = _np.ascontiguousarray(inputs[name])
        arrays[f"in_{name}"] = a
        args.append(nc.dram_tensor(f"in_{name}", a.shape, _mybir.dt.from_np(a.dtype), kind="ExternalInput").ap())
    c = _np.zeros((P, C_END), _np.float32)
    c[:, C_ID:C_ID + P] = _np.eye(P)
    c[:, C_IOTA:C_IOTA + J * WIN] = _np.tile(_np.arange(WIN), J)
    c[:, C_PMOD] = _np.arange(P) % WIN
    c[0:3, C_MASK:C_MASK + 3] = _np.eye(3)
    arrays["in_consts"] = c
    args.append(nc.dram_tensor("in_consts", c.shape, _mybir.dt.from_np(c.dtype), kind="ExternalInput").ap())
    args.append(nc.dram_tensor("out_0", (N, O), F32, kind="ExternalOutput").ap())
    build(nc, *args)
    r = _run(nc, [arrays], core_ids=[0])
    return r.results[0]["out_0"]
```
